# Optimizing a Trainium2 kernel written in Bass

```python
import numpy as np
import jax
import jax.numpy as jnp

def _softmax(x, axis=-1):
    return jax.nn.softmax(x, axis=axis)

def _gelu(x):
    return jax.nn.gelu(x, approximate=True)

def _silu(x):
    return jax.nn.silu(x)

def _sigmoid(x):
    return jax.nn.sigmoid(x)

def _layernorm(x, axis=-1, eps=1e-05):
    m = jnp.mean(x, axis=axis, keepdims=True)
    v = jnp.var(x, axis=axis, keepdims=True)
    return (x - m) / jnp.sqrt(v + eps)

def _scatter_add(tgt, idx, src, axis=0):
    return tgt.at[idx].add(src)

def _segment_sum(src, seg, n):
    return jax.ops.segment_sum(src, seg, n)
kernel_name = 'mk_gnn_preln_d1_gnn_r8_e85c33'

def setup_inputs(seed: int=0):
    np.random.seed(seed)
    _w = jnp.asarray

    def _rec_inputs():
        import jax
        import jax.numpy as jnp
        _gk = jax.random.key(seed)
        x = -6.415e-05 + 1 * jax.random.normal(jax.random.fold_in(_gk, 1), (1250, 1024), jnp.float32)
        src = jax.random.randint(jax.random.fold_in(_gk, 2), (20000,), 0, 1250, jnp.int32)
        dst = jax.random.randint(jax.random.fold_in(_gk, 3), (20000,), 0, 1250, jnp.int32)
        _o = jnp.argsort(dst, stable=True)
        src = src[_o]
        dst = dst[_o]
        edge_type_8 = jax.random.randint(jax.random.fold_in(_gk, 12), (20000,), 0, 8, jnp.int32)
        return (x, src, dst, edge_type_8)
    x, src, dst, edge_type_8 = _rec_inputs()

    def _L0_gnn_setup():
        import jax, jax.numpy as jnp
        import numpy as np
        N, D, R, E = (1250, 1024, 8, 10000)

        def _rgcn(x, edge_index, edge_type, weight, root, bias):
            src, dst = (edge_index[0], edge_index[1])
            msgs = x[src]
            out = x @ root + bias
            n = x.shape[0]
            for r in range(weight.shape[0]):
                mask = (edge_type == r).astype(x.dtype)
                sums = jax.ops.segment_sum(msgs * mask[:, None], dst, num_segments=n)
                cnt = jax.ops.segment_sum(mask, dst, num_segments=n)
                mean = sums / jnp.maximum(cnt, 1.0)[:, None]
                out = out + mean @ weight[r]
            return out
        key = jax.random.key(seed)
        ks = jax.random.split(key, 8)
        s = 1.0 / np.sqrt(D)
        x = jax.random.normal(ks[0], (N, D), dtype=jnp.float32)
        edge_index = jax.random.randint(ks[1], (2, E), 0, N, dtype=jnp.int64)
        edge_type = jax.random.randint(ks[2], (E,), 0, R, dtype=jnp.int64)
        weight = jax.random.normal(ks[3], (R, D, D), dtype=jnp.float32) * s
        root = jax.random.normal(ks[4], (D, D), dtype=jnp.float32) * s
        bias = jnp.zeros((D,), dtype=jnp.float32)
        w_gate = jax.random.normal(ks[5], (2 * D, D), dtype=jnp.float32) * (1.0 / np.sqrt(2 * D))
        b_gate = jnp.zeros((D,), dtype=jnp.float32)
        return {'x': x, 'edge_index': edge_index, 'edge_type': edge_type, 'weight': weight, 'root': root, 'bias': bias, 'w_gate': w_gate, 'b_gate': b_gate}
    _L0_gnn_all = _L0_gnn_setup()
    _L0_gnn_in = {k: v for k, v in _L0_gnn_all.items() if k in ('weight', 'root', 'bias', 'w_gate', 'b_gate')}
    del _L0_gnn_all
    return {'x': x, 'src': src, 'dst': dst, 'edge_type_8': edge_type_8, 'L0_gnn_weight': _L0_gnn_in['weight'], 'L0_gnn_root': _L0_gnn_in['root'], 'L0_gnn_bias': _L0_gnn_in['bias'], 'L0_gnn_w_gate': _L0_gnn_in['w_gate'], 'L0_gnn_b_gate': _L0_gnn_in['b_gate']}

def reference(x, src, dst, edge_type_8, L0_gnn_weight, L0_gnn_root, L0_gnn_bias, L0_gnn_w_gate, L0_gnn_b_gate):
    import jax
    import jax.numpy as jnp

    def _L0_gnn_ref(x, edge_index, edge_type, weight, root, bias, w_gate, b_gate):
        import jax, jax.numpy as jnp
        import numpy as np
        N, D, R, E = (1250, 1024, 8, 10000)

        def _rgcn(x, edge_index, edge_type, weight, root, bias):
            src, dst = (edge_index[0], edge_index[1])
            msgs = x[src]
            out = x @ root + bias
            n = x.shape[0]
            for r in range(weight.shape[0]):
                mask = (edge_type == r).astype(x.dtype)
                sums = jax.ops.segment_sum(msgs * mask[:, None], dst, num_segments=n)
                cnt = jax.ops.segment_sum(mask, dst, num_segments=n)
                mean = sums / jnp.maximum(cnt, 1.0)[:, None]
                out = out + mean @ weight[r]
            return out
        u = _rgcn(x, edge_index, edge_type, weight, root, bias)
        z = jnp.concatenate([u, x], axis=1) @ w_gate + b_gate
        h = jnp.tanh(u) * z + x * (1.0 - z)
        return h
    edge_index = jnp.stack([src, dst])
    h = jnp.maximum(_layernorm(x, axis=-1), 0.0)
    x = x + _L0_gnn_ref(h, edge_index, edge_type_8, L0_gnn_weight, L0_gnn_root, L0_gnn_bias, L0_gnn_w_gate, L0_gnn_b_gate)
    return x

_drawn_inputs = setup_inputs


def setup_inputs(seed=0):
    import zlib

    import numpy as np

    out = dict(_drawn_inputs(seed))
    spreads = {'L0_gnn_bias': (0.0, 0.1), 'L0_gnn_b_gate': (0.0, 0.1)}
    factors = {}
    for name, (base, spread) in spreads.items():
        noise = np.random.default_rng([zlib.crc32(name.encode()), seed]).standard_normal(out[name].shape)
        drawn = base * np.exp(spread * noise) if base else spread * noise
        out[name] = jnp.asarray(drawn.astype(out[name].dtype))
    for name, factor in factors.items():
        out[name] = (out[name] * factor).astype(out[name].dtype)
    return out
```

```python
from contextlib import ExitStack

import concourse.bass as bass
from concourse import mybir

F32 = mybir.dt.float32
F16 = mybir.dt.float16
BF16 = mybir.dt.bfloat16
I32 = mybir.dt.int32
U16 = mybir.dt.uint16
ALU = mybir.AluOpType
ACT = mybir.ActivationFunctionType
AX = mybir.AxisListType

P = 128
ROUND = 1.5 * 2.0 ** 23
H_SCALE = 1024.0


def gated_rgcn_preln(nc, x, src, dst, edge_type, weight, root, bias, w_gate, b_gate, out):
    N, D = x.shape
    R = weight.shape[0]
    E = src.shape[0]
    KT = D // P
    EP = 125
    EC = E // EP
    DT = 125
    NJ = N // DT
    NG = R * NJ
    TMAX = 320
    assert EP * EC == E and NJ * DT == N and 2 * NG + E // P + 1 + 4 <= TMAX + 2
    RING = 4
    LT = [(i * P, min(P, N - i * P)) for i in range((N + P - 1) // P)]
    NB = [(0, 4), (4, 4), (8, 2)]
    NCOL = [(a * DT, c * DT) for a, c in NB]
    NU = len(NB) * KT
    FB = [(0, 512), (512, 512), (1024, N - 1024)]
    GC = 3
    GCH = [(g, min(GC, NG - g)) for g in range(0, NG, GC)]
    HC = 512

    h_rows = nc.dram_tensor("h_rows", [N, 2 * D], F16).ap()
    mean_t = nc.dram_tensor("mean_t", [NG, P, KT * DT], F32).ap()

    ctx = ExitStack()
    with ctx:
        def sb(name, shape, dt):
            return ctx.enter_context(nc.sbuf_tensor(name, shape, dt))

        def sem(name):
            return ctx.enter_context(nc.semaphore(name))

        hT = sb("hT", [P, KT, N], F32)
        uT = sb("uT", [P, KT, N], F32)
        W = sb("W", [P, 2, KT * D], F32)
        M = sb("M", [P, NJ * KT * DT], F32)
        G = sb("G", [P, RING, 2 * D], F16)
        ident = sb("ident", [P, P], F32)
        ones_bf = sb("ones_bf", [P, P], BF16)
        before = sb("before", [P, P], BF16)
        upper = sb("upper", [NG, NG + 1], BF16)
        ones_h = sb("ones_h", [P, 2], F16)
        iota_t = sb("iota_t", [P, TMAX], F16)
        iota_d = sb("iota_d", [P, DT], F16)
        edge_src = sb("edge_src", [P, TMAX], I32)
        neg_dst = sb("neg_dst", [P, TMAX], F32)
        idx = sb("idx", [P, RING, 1], I32)
        onehot = sb("onehot", [P, RING, P], F16)
        absd = sb("absd", [P, 2, DT], F16)
        bounds = sb("bounds", [P, NG + 2], I32)
        bias_t = sb("bias_t", [P, KT], F32)
        bgate_t = sb("bgate_t", [P, KT], F32)
        stats = sb("stats", [P, 2, 2, 6], F32)
        mv = sb("mv", [P, 2, 2], F32)
        sd = sb("sd", [P, 2, 4], F32)
        inv = sb("inv", [P, 2, 2], F32)

        xbuf = G[:, 0:2, :].bitcast(F32)
        hbuf = G[:, 2:4, :].bitcast(F32)
        SCAN = NG * EC
        scan = M[:, 0:SCAN // 2].bitcast(BF16)
        scan_u = M[:, 0:SCAN // 2].bitcast(U16)
        at = SCAN // 2
        hilo = M[:, at:at + 2 * D].bitcast(F16).rearrange("p (b n) -> p b n", b=2)
        at += 2 * D
        lo_hot = M[:, at:at + 4 * P // 2].bitcast(F16).rearrange("p (b n) -> p b n", b=4)
        at += 4 * P // 2
        hi_val = M[:, at:at + 4 * TMAX].bitcast(F16).rearrange("p (b v n) -> p b v n", b=4, v=2)
        assert at + 4 * TMAX <= NJ * KT * DT
        hot = W[:, 1, 0:SCAN // 2].bitcast(BF16)
        at = SCAN // 2
        ework = W[:, 1, at:at + 11 * EC].rearrange("p (b n) -> p b n", b=11)
        assert at + 11 * EC <= KT * D
        src_i, dst_i, typ_i = (ework[0:EP, b, :].bitcast(I32) for b in range(3))
        src_f, dst_f, typ_f, grp, dst1, key, pos, hi_t, = (ework[0:EP, b, :] for b in range(3, 11))
        lo_t = typ_f
        iota_g = mv_iota = sb("iota_g", [P, NG], F32)
        tstart = sb("tstart", [P, NG], F32)
        ntile = sb("ntile", [NG, 4], F32)
        ltile = sb("ltile", [NG, P], BF16)
        natn = M[:, 0:2 * D].rearrange("p (b n) -> p b n", b=2)
        accT = M[:, 2 * D:2 * D + 2 * KT * DT].rearrange("p (b n) -> p b n", b=2)
        wbot = M[:, 0:KT * D].rearrange("p (k n) -> p k n", k=KT)
        gT = W[:, 0, 0:KT * HC].rearrange("p (k n) -> p k n", k=KT)
        xres = W[:, 0, KT * HC:KT * HC + 2 * D].rearrange("p (b n) -> p b n", b=2)
        obuf = W[:, 0, KT * HC + 2 * D:KT * HC + 4 * D].rearrange("p (b n) -> p b n", b=2)
        tanh_u = G[:, 0:2, 0:2 * HC].bitcast(F32)
        diff = G[:, 2:4, 0:2 * HC].bitcast(F32)

        ps = ctx.enter_context(nc.psum_tensor("ps", [P, 8, 512], F32))

        s = {n: sem(n) for n in (
            "consts", "consts0", "edges_loaded", "x_loaded0", "x_loaded1", "bias_loaded", "w_loaded0", "w_loaded1",
            "bot_loaded", "var_ready", "sd_ready", "scale_ready", "h_ready", "hi_ready", "hilo_ready", "rows_stored0",
            "rows_stored1", "lnT_done", "hT_ready", "u_done", "root_evac", "dve_step", "scan_ready", "totals_done",
            "ltile_ready", "bounds_done", "bounds_ready", "rank_done", "rank_used", "step_ready", "step_used",
            "table_done", "table_ready", "idx_ready", "gathered0", "gathered1", "gathered2", "gathered3", "abs_ready",
            "tile_ready", "tile_done", "inv_step", "natn_ready", "meanT_done", "meanT_ready", "mean_stored0",
            "mean_stored1", "mean_loaded0", "mean_loaded1", "mean_loaded2", "main_done", "u_added",
            "z_done", "tanh_ready", "diff_ready", "prod_ready", "gate_ready", "gateT_done", "res_ready",
            "xres_loaded0", "xres_loaded1", "out_stored0", "out_stored1", "ring_clear")}

        block = ctx.enter_context(nc.Block())

        def store_out(sp, i):
            n0, rows = LT[i]
            sp.wait_ge(s["res_ready"], i + 1)
            sp.dma_start(out[n0:n0 + rows, :], obuf[0:rows, i % 2, :]).then_inc(s[f"out_stored{i % 2}"], 16)

        def copy_hT(act, i):
            n0, rows = LT[i]
            act.wait_ge(s["lnT_done"], i + 1)
            b = 2 * (i % 2)
            nc.scalar.activation(hT[:, :, n0:n0 + rows],
                                 ps[:, b:b + 2, :].rearrange("p b (k n) -> p (b k) n", n=P)[:, :, 0:rows],
                                 ACT.Copy).then_inc(s["hT_ready"], 1)

        def root_bank(n, m):
            return m if n < 2 else 2 + m % 6

        @block.sync
        def _(sp):
            sp.dma_start(dst_i, dst.rearrange("(p c) -> p c", p=EP)).then_inc(s["edges_loaded"], 16)
            sp.dma_start(typ_i, edge_type.rearrange("(p c) -> p c", p=EP)).then_inc(s["edges_loaded"], 16)
            sp.dma_start(src_i, src.rearrange("(p c) -> p c", p=EP)).then_inc(s["edges_loaded"], 16)

            def load_x(i):
                n0, rows = LT[i]
                sp.dma_start(xbuf[0:rows, i % 2, :], x[n0:n0 + rows, :]).then_inc(s[f"x_loaded{i % 2}"], 16)

            load_x(0)
            load_x(1)
            sp.dma_start(bias_t[:, :], bias.rearrange("(k p) -> p k", p=P), allow_slow_non_contiguous=True).then_inc(s["bias_loaded"], 16)
            sp.dma_start(bgate_t[:, :], b_gate.rearrange("(k p) -> p k", p=P), allow_slow_non_contiguous=True).then_inc(s["bias_loaded"], 16)
            sp.dma_start(W[:, 0, :].rearrange("p (k n) -> p k n", k=KT),
                         root.rearrange("(k p) n -> p k n", p=P)).then_inc(s["w_loaded0"], 16)
            for i, (n0, rows) in enumerate(LT):
                if i + 2 < len(LT):
                    sp.wait_ge(s["h_ready"], i + 1)
                    load_x(i + 2)
                sp.wait_ge(s["hilo_ready"], i + 1)
                sp.dma_start(h_rows[n0:n0 + rows, :], hilo[0:rows, i % 2, :]).then_inc(s[f"rows_stored{i % 2}"], 16)
            sp.wait_ge(s["table_ready"], 1)
            sp.dma_start(W[:, 1, :].rearrange("p (k n) -> p k n", k=KT),
                         weight[0].rearrange("(k p) n -> p k n", p=P)).then_inc(s["w_loaded1"], 16)
            with sp.Fori(0, NG // 2) as gp:
                for b in range(2):
                    sp.wait_ge(s["meanT_ready"], gp * 2 + (b + 1))
                    sp.dma_start(mean_t[bass.ds(gp * 2 + b, 1)].rearrange("a p n -> p (a n)"),
                                 accT[:, b, :]).then_inc(s[f"mean_stored{b}"], 16)
            for b in range(2):
                sp.wait_ge(s[f"mean_stored{b}"], 16 * (NG // 2))

            def load_mean(r, n):
                a, c = NB[n]
                dst_ap = M[:, a * KT * DT:(a + c) * KT * DT].rearrange("p (j n) -> p j n", j=c)
                src_ap = mean_t[bass.ds(r * NJ + a, c)].rearrange("j p n -> p j n")
                sp.dma_start(dst_ap, src_ap).then_inc(s[f"mean_loaded{n}"], 16)

            def load_w(r, b):
                sp.dma_start(W[:, b, :].rearrange("p (k n) -> p k n", k=KT),
                             weight[bass.ds(r, 1)].rearrange("a (k p) n -> p (a k) n", p=P)).then_inc(s[f"w_loaded{b}"], 16)

            sp.wait_ge(s["root_evac"], NU)
            for n in range(len(NB)):
                load_mean(0, n)
            load_w(1, 0)
            with sp.Fori(0, R // 2 - 1) as rp:
                for n in range(len(NB)):
                    sp.wait_ge(s["main_done"], rp * (2 * NU) + (n + 1) * KT)
                    load_mean(rp * 2 + 1, n)
                load_w(rp * 2 + 2, 1)
                for n in range(len(NB)):
                    sp.wait_ge(s["main_done"], rp * (2 * NU) + (NU + (n + 1) * KT))
                    load_mean(rp * 2 + 2, n)
                load_w(rp * 2 + 3, 0)
            done = (R - 2) * NU
            for n in range(len(NB)):
                sp.wait_ge(s["main_done"], done + (n + 1) * KT)
                load_mean(R - 1, n)
            sp.dma_start(W[:, 1, :].rearrange("p (k n) -> p k n", k=KT),
                         w_gate[0:D, :].rearrange("(k p) n -> p k n", p=P)).then_inc(s["w_loaded1"], 16)
            done += NU
            sp.wait_ge(s["main_done"], done + 2 * KT)
            bot = w_gate[D:2 * D, :].rearrange("(k p) n -> p k n", p=P)
            sp.dma_start(wbot[:, 0:KT - 1, :], bot[:, 0:KT - 1, :]).then_inc(s["bot_loaded"], 16)
            sp.wait_ge(s["main_done"], done + NU)
            sp.dma_start(wbot[:, KT - 1, :], bot[:, KT - 1, :]).then_inc(s["bot_loaded"], 16)

            for i, (n0, rows) in enumerate(LT):
                if i >= 2:
                    sp.wait_ge(s["res_ready"], i - 1)
                sp.dma_start(xres[0:rows, i % 2, :], x[n0:n0 + rows, :]).then_inc(s[f"xres_loaded{i % 2}"], 16)
                if i >= 1:
                    store_out(sp, i - 1)
            store_out(sp, len(LT) - 1)
            sp.wait_ge(s["out_stored0"], 16 * ((len(LT) + 1) // 2))
            sp.wait_ge(s["out_stored1"], 16 * (len(LT) // 2))

        @block.gpsimd
        def _(pool):
            pool.memset(ident[:, :], 0.0).then_inc(s["consts0"], 1)
            pool.memset(ones_bf[:, :], 1.0).then_inc(s["consts0"], 1)
            pool.memset(before[:, :], 0.0).then_inc(s["consts0"], 1)
            pool.memset(upper[:, :], 1.0).then_inc(s["consts0"], 1)
            pool.memset(ones_h[:, :], 1.0).then_inc(s["consts0"], 1)
            pool.wait_ge(s["consts0"], 5)
            pool.affine_select(out=ident[:, :], in_=ident[:, :], compare_op=ALU.not_equal, fill=1.0, base=0,
                               pattern=[[-1, P]], channel_multiplier=1).then_inc(s["consts"], 1)
            pool.affine_select(out=before[:, :], in_=before[:, :], compare_op=ALU.is_gt, fill=-1.0, base=0,
                               pattern=[[1, P]], channel_multiplier=-1).then_inc(s["consts"], 1)
            pool.affine_select(out=upper[:, :], in_=upper[:, :], compare_op=ALU.is_gt, fill=0.0, base=0,
                               pattern=[[1, NG + 1]], channel_multiplier=-1).then_inc(s["consts"], 1)
            pool.iota(iota_t[:, :], pattern=[[1, TMAX]], base=0, channel_multiplier=0,
                      allow_small_or_imprecise_dtypes=True).then_inc(s["consts"], 1)
            pool.iota(iota_d[:, :], pattern=[[1, DT]], base=1, channel_multiplier=0,
                      allow_small_or_imprecise_dtypes=True).then_inc(s["consts"], 1)
            pool.iota(iota_g[:, :], pattern=[[1, NG]], base=0, channel_multiplier=0,
                      allow_small_or_imprecise_dtypes=True).then_inc(s["consts"], 1)

            pool.wait_ge(s["lnT_done"], len(LT))
            pool.wait_ge(s["hilo_ready"], len(LT))
            pool.memset(G[:, :, :], 0.0).then_inc(s["ring_clear"], 1)
            pool.wait_ge(s["ring_clear"], 1)
            for b in range(2):
                pool.wait_ge(s[f"rows_stored{b}"], 16 * (len(LT) // 2))
            pool.wait_ge(s["table_ready"], 1)
            turns = pool.value_load(bounds[0:1, NG + 1:NG + 2], min_val=2 * NG // RING, max_val=TMAX // RING)

            last_row = pool.alloc_register("last_row")
            pool.reg_mov(last_row, N - 1)

            def gather(t, b):
                pool.tensor_copy(idx[:, b, :], edge_src[:, bass.ds(t, 1)]).then_inc(s["idx_ready"], 1)
                pool.wait_ge(s["idx_ready"], t + 1)
                pool.reg_alu(last_row, last_row, N - 1, ALU.min)
                pool.indirect_dma_start(out=G[:, b, :], out_offset=None, in_=h_rows,
                                        in_offset=bass.IndirectOffsetOnAxis(ap=idx[:, b, :], axis=0),
                                        bounds_check=last_row, oob_is_err=False).then_inc(s[f"gathered{b}"], 16)

            for b in range(RING):
                gather(b, b)
            with pool.Fori(1, turns) as q:
                for b in range(RING):
                    pool.wait_ge(s["tile_done"], q * RING + (b - RING + 1))
                    gather(pool.snap(q * RING + b), b)

        @block.scalar
        def _(act):
            act.wait_ge(s["consts"], 6)
            for i, (n0, rows) in enumerate(LT):
                b = i % 2
                act.wait_ge(s["var_ready"], i + 1)
                nc.scalar.activation(sd[0:rows, b, 0:1], sd[0:rows, b, 3:4], ACT.Sqrt).then_inc(s["sd_ready"], 1)
                act.wait_ge(s["scale_ready"], i + 1)
                if i >= 2:
                    act.wait_ge(s["lnT_done"], i - 1)
                    act.wait_ge(s["hilo_ready"], i - 1)
                    act.wait_ge(s[f"rows_stored{b}"], 16 * (i // 2))
                nc.scalar.activation(hbuf[0:rows, b, :], xbuf[0:rows, b, :], ACT.Relu, bias=sd[0:rows, b, 2:3],
                                     scale=sd[0:rows, b, 1:2]).then_inc(s["h_ready"], 1)
                act.wait_ge(s["h_ready"], i + 1)
                nc.scalar.activation(hilo[0:rows, b, 0:D], hbuf[0:rows, b, :], ACT.Copy,
                                     scale=H_SCALE).then_inc(s["hi_ready"], 1)
                if i >= 1:
                    copy_hT(act, i - 1)
            copy_hT(act, len(LT) - 1)

            act.wait_ge(s["bias_loaded"], 32)
            for q in range(NU):
                n, m = divmod(q, KT)
                c0, cols = NCOL[n]
                act.wait_ge(s["u_done"], q + 1)
                nc.scalar.activation(uT[:, m, c0:c0 + cols], ps[:, root_bank(n, m), 0:cols], ACT.Identity,
                                     bias=bias_t[:, m:m + 1]).then_inc(s["root_evac"], 1)

            act.wait_ge(s["table_ready"], 1)
            turns = act.value_load(bounds[0:1, NG + 1:NG + 2], min_val=2 * NG // RING, max_val=TMAX // RING)

            def make_onehot(t, b, landed):
                nc.scalar.activation(absd[:, b % 2, :], iota_d[:, :], ACT.Abs,
                                     bias=neg_dst[:, bass.ds(t, 1)]).then_inc(s["abs_ready"], 1)
                act.wait_ge(s["abs_ready"], t + 1)
                act.wait_ge(s[f"gathered{b}"], landed)
                nc.scalar.activation(onehot[:, b, 0:DT], absd[:, b % 2, :], ACT.Relu, bias=1.0,
                                     scale=-1.0).then_inc(s["tile_ready"], 1)

            for b in range(RING):
                make_onehot(b, b, 16)
            with act.Fori(1, turns) as q:
                for b in range(RING):
                    act.wait_ge(s["tile_done"], q * RING + (b - RING + 1))
                    make_onehot(q * RING + b, b, q * 16 + 16)

            act.wait_ge(s["u_added"], R * NU)
            for q in range(len(FB) * KT):
                n, m = divmod(q, KT)
                c0, cols = FB[n]
                if q >= 2:
                    act.wait_ge(s["diff_ready"], q - 1)
                nc.scalar.activation(tanh_u[:, q % 2, 0:cols], uT[:, m, c0:c0 + cols],
                                     ACT.Tanh).then_inc(s["tanh_ready"], 1)

        @block.vector
        def _(dve):
            steps = [0]

            def step(ins):
                steps[0] += 1
                ins.then_inc(s["dve_step"], 1)
                dve.wait_ge(s["dve_step"], steps[0])

            def split_low(i):
                rows = LT[i][1]
                dve.wait_ge(s["hi_ready"], i + 1)
                nc.vector.scalar_tensor_tensor(out=hilo[0:rows, i % 2, D:2 * D], in0=hbuf[0:rows, i % 2, :],
                                               scalar=H_SCALE, in1=hilo[0:rows, i % 2, 0:D], op0=ALU.mult,
                                               op1=ALU.subtract).then_inc(s["hilo_ready"], 1)

            for i, (n0, rows) in enumerate(LT):
                b = i % 2
                dve.wait_ge(s[f"x_loaded{b}"], 16 * (i // 2 + 1))
                if i >= 2:
                    dve.wait_ge(s["h_ready"], i - 1)
                nc.vector.bn_stats(stats[0:rows, b, 0, :], xbuf[0:rows, b, 0:512])
                step(nc.vector.bn_stats(stats[0:rows, b, 1, :], xbuf[0:rows, b, 512:1024]))
                step(nc.vector.bn_aggr(mv[0:rows, b, :], stats[0:rows, b, :, :].rearrange("p a f -> p (a f)")))
                nc.vector.tensor_scalar(sd[0:rows, b, 3:4], mv[0:rows, b, 1:2], 1e-5, None,
                                        ALU.add).then_inc(s["var_ready"], 1)
                dve.wait_ge(s["sd_ready"], i + 1)
                step(nc.vector.reciprocal(sd[0:rows, b, 1:2], sd[0:rows, b, 0:1]))
                nc.vector.scalar_tensor_tensor(out=sd[0:rows, b, 2:3], in0=mv[0:rows, b, 0:1], scalar=-1.0,
                                               in1=sd[0:rows, b, 1:2], op0=ALU.mult,
                                               op1=ALU.mult).then_inc(s["scale_ready"], 1)
                if i >= 1:
                    split_low(i - 1)
            split_low(len(LT) - 1)

            dve.wait_ge(s["edges_loaded"], 48)
            dve.wait_ge(s["consts"], 6)
            nc.vector.tensor_copy(src_f, src_i)
            nc.vector.tensor_copy(typ_f, typ_i)
            step(nc.vector.tensor_copy(dst_f, dst_i))
            step(nc.vector.tensor_scalar(grp, dst_f, -(DT - 1) / 2, 1.0 / DT, ALU.add, ALU.mult))
            step(nc.vector.tensor_scalar(grp, grp, ROUND, None, ALU.add))
            step(nc.vector.tensor_scalar(grp, grp, -ROUND, None, ALU.add))
            step(nc.vector.scalar_tensor_tensor(out=dst1, in0=grp, scalar=-float(DT), in1=dst_f, op0=ALU.mult, op1=ALU.add))
            step(nc.vector.tensor_scalar(dst1, dst1, 1.0, None, ALU.add))
            step(nc.vector.scalar_tensor_tensor(out=key, in0=typ_f, scalar=float(NJ), in1=grp, op0=ALU.mult, op1=ALU.add))
            hot3 = hot[0:EP].rearrange("p (g c) -> p g c", g=NG)
            scan3 = scan[0:EP].rearrange("p (g c) -> p g c", g=NG)
            pos3 = scan_u[0:EP].rearrange("p (g c) -> p g c", g=NG)
            nc.vector.tensor_tensor(hot3, key.unsqueeze(1).to_broadcast([EP, NG, EC]),
                                    iota_g[0:EP, :].unsqueeze(2).to_broadcast([EP, NG, EC]), ALU.is_equal)
            step(nc.vector.memset(scan[0:EP, :], 1.0))
            step(nc.vector.memset(scan3[:, :, 0:1], 0.0))
            nc.vector.tensor_tensor_scan(out=scan[0:EP, :], data0=scan[0:EP, :], data1=hot[0:EP, :], initial=0.0,
                                         op0=ALU.mult, op1=ALU.add).then_inc(s["scan_ready"], 1)

            dve.wait_ge(s["totals_done"], 1)
            step(nc.vector.tensor_scalar(ntile[:, 0:1], ps[0:NG, 0, 0:1], (P - 1) / 2, 1.0 / P, ALU.add, ALU.mult))
            step(nc.vector.tensor_scalar(ntile[:, 1:2], ntile[:, 0:1], ROUND, None, ALU.add))
            step(nc.vector.tensor_scalar(ntile[:, 2:3], ntile[:, 1:2], -ROUND, 2.0, ALU.add, ALU.max))
            nc.vector.tensor_scalar(ltile[:, :], ones_bf[0:NG, :], ntile[:, 2:3], None,
                                    ALU.mult).then_inc(s["ltile_ready"], 1)
            dve.wait_ge(s["bounds_done"], 1)
            nc.vector.tensor_copy(bounds[:, 0:NG], ps[:, 1, 0:NG])
            step(nc.vector.tensor_scalar(inv[:, 0, 0:1], ps[:, 1, NG:NG + 1], (RING - 1) / 2, 1.0 / RING, ALU.add, ALU.mult))
            step(nc.vector.tensor_scalar(inv[:, 0, 1:2], inv[:, 0, 0:1], ROUND, None, ALU.add))
            step(nc.vector.tensor_scalar(inv[:, 1, 0:1], inv[:, 0, 1:2], -ROUND, None, ALU.add))
            nc.vector.tensor_copy(bounds[:, NG + 1:NG + 2], inv[:, 1, 0:1])
            nc.vector.tensor_scalar(bounds[:, NG:NG + 1], inv[:, 1, 0:1], float(RING), None, ALU.mult)
            step(nc.vector.tensor_scalar(tstart[:, :], ps[:, 1, 0:NG], float(P), None, ALU.mult))
            dve.wait_ge(s["dve_step"], steps[0])
            for ch, (g0, gn) in enumerate(GCH):
                dve.wait_ge(s["rank_done"], ch + 1)
                for g in range(g0, g0 + gn):
                    last = nc.vector.scalar_tensor_tensor(
                        out=pos3[:, g, :], in0=ps[0:EP, 2 + ch % 6, (g - g0) * EC:(g - g0 + 1) * EC],
                        scalar=tstart[0:EP, g:g + 1], in1=hot3[:, g, :], op0=ALU.add, op1=ALU.mult)
                last.then_inc(s["rank_used"], 1)
            dve.wait_ge(s["rank_used"], len(GCH))
            step(nc.vector.tensor_reduce(pos, pos3.rearrange("p g c -> p c g"), AX.X, ALU.add))
            step(nc.vector.tensor_scalar(hi_t, pos, -(P - 1) / 2, 1.0 / P, ALU.add, ALU.mult))
            step(nc.vector.tensor_scalar(hi_t, hi_t, ROUND, None, ALU.add))
            step(nc.vector.tensor_scalar(hi_t, hi_t, -ROUND, None, ALU.add))
            step(nc.vector.scalar_tensor_tensor(out=lo_t, in0=hi_t, scalar=-float(P), in1=pos, op0=ALU.mult, op1=ALU.add))

            def table_step(c, b):
                nc.vector.tensor_scalar(lo_hot[0:EP, b, :], iota_t[0:EP, 0:P], lo_t[:, bass.ds(c, 1)], None, ALU.is_equal)
                nc.vector.tensor_scalar(hi_val[0:EP, b, 0, :], iota_t[0:EP, :], hi_t[:, bass.ds(c, 1)],
                                        src_f[:, bass.ds(c, 1)], ALU.is_equal, ALU.mult)
                nc.vector.tensor_scalar(hi_val[0:EP, b, 1, :], iota_t[0:EP, :], hi_t[:, bass.ds(c, 1)],
                                        dst1[:, bass.ds(c, 1)], ALU.is_equal, ALU.mult).then_inc(s["step_ready"], 1)

            for b in range(4):
                table_step(b, b)
            with dve.Fori(1, EC // 4) as q:
                for b in range(4):
                    dve.wait_ge(s["step_used"], q * 4 + (b - 3))
                    table_step(q * 4 + b, b)
            dve.wait_ge(s["table_done"], 1)
            nc.vector.tensor_scalar(neg_dst[:, :], ps[:, 1, 0:TMAX], -1.0, None, ALU.mult)
            step(nc.vector.tensor_scalar(iota_t[:, :], ps[:, 1, 0:TMAX], 0.0, 2.0 * P * 8, ALU.is_equal, ALU.mult))
            nc.vector.tensor_tensor(edge_src[:, :], ps[:, 0, 0:TMAX], iota_t[:, :], ALU.add).then_inc(s["table_ready"], 1)
            dve.wait_ge(s["table_ready"], 1)

            def mean_rows(g, b, first):
                end = dve.value_load(bounds[0:1, bass.ds(g + 1, 1)], min_val=2, max_val=TMAX - RING)
                dve.wait_ge(s["tile_done"], end)
                nc.vector.tensor_scalar(inv[0:DT, b, 0:1], ps[0:DT, 4 + 3 * b, 0:1], 1.0, H_SCALE, ALU.max,
                                        ALU.mult).then_inc(s["inv_step"], 1)
                dve.wait_ge(s["inv_step"], g * 2 + 1)
                nc.vector.reciprocal(inv[0:DT, b, 1:2], inv[0:DT, b, 0:1]).then_inc(s["inv_step"], 1)
                dve.wait_ge(s["inv_step"], g * 2 + 2)
                if not first:
                    dve.wait_ge(s["meanT_done"], g - 1)
                nc.vector.tensor_scalar(natn[0:DT, b, :], ps[0:DT, 2 * b:2 * b + 2, :].rearrange("p b n -> p (b n)"),
                                        inv[0:DT, b, 1:2], None, ALU.mult).then_inc(s["natn_ready"], 1)

            def mean_cols(g, b, stored):
                dve.wait_ge(s["meanT_done"], g + 1)
                if stored is not None:
                    dve.wait_ge(s[f"mean_stored{b}"], stored)
                nc.vector.tensor_copy(accT[:, b, :].rearrange("p (b n) -> p b n", b=2),
                                      ps[:, 5:7, 0:KT * DT // 2]).then_inc(s["meanT_ready"], 1)

            mean_rows(0, 0, True)
            mean_rows(1, 1, True)
            mean_cols(0, 0, None)
            mean_rows(2, 0, False)
            mean_cols(1, 1, None)
            mean_rows(3, 1, False)
            with dve.Fori(2, NG // 2) as gp:
                mean_cols(gp * 2 - 2, 0, (gp - 1) * 16)
                mean_rows(gp * 2, 0, False)
                mean_cols(gp * 2 - 1, 1, (gp - 1) * 16)
                mean_rows(gp * 2 + 1, 1, False)
            mean_cols(NG - 2, 0, 16 * (NG // 2 - 1))
            mean_cols(NG - 1, 1, 16 * (NG // 2 - 1))

            dve.wait_ge(s["root_evac"], NU)
            with dve.Fori(0, R) as r:
                for q in range(NU):
                    n, m = divmod(q, KT)
                    c0, cols = NCOL[n]
                    u = uT[:, m, c0:c0 + cols]
                    dve.wait_ge(s["main_done"], r * NU + (q + 1))
                    nc.vector.tensor_tensor(u, ps[:, m, 0:cols], u, ALU.add).then_inc(s["u_added"], 1)

            dve.wait_ge(s["u_added"], R * NU)
            for n, (c0, cols) in enumerate(FB):
                for m in range(KT):
                    q = n * KT + m
                    h = hT[:, m, c0:c0 + cols]
                    dve.wait_ge(s["tanh_ready"], q + 1)
                    nc.vector.tensor_tensor(diff[:, q % 2, 0:cols], tanh_u[:, q % 2, 0:cols], h,
                                            ALU.subtract).then_inc(s["diff_ready"], 1)
                    dve.wait_ge(s["diff_ready"], q + 1)
                    dve.wait_ge(s["z_done"], q + 1)
                    nc.vector.scalar_tensor_tensor(out=diff[:, q % 2, 0:cols], in0=ps[:, m % 4, 0:cols],
                                                   scalar=bgate_t[:, m:m + 1], in1=diff[:, q % 2, 0:cols],
                                                   op0=ALU.add, op1=ALU.mult).then_inc(s["prod_ready"], 1)
                    dve.wait_ge(s["prod_ready"], q + 1)
                    if n and m == 0:
                        dve.wait_ge(s["gateT_done"], (c0 + P - 1) // P)
                    nc.vector.tensor_tensor(gT[:, m, 0:cols], diff[:, q % 2, 0:cols], h, ALU.add).then_inc(s["gate_ready"], 1)
                for i in range(c0 // P, (c0 + cols + P - 1) // P):
                    rows = LT[i][1]
                    dve.wait_ge(s["gateT_done"], i + 1)
                    dve.wait_ge(s[f"xres_loaded{i % 2}"], 16 * (i // 2 + 1))
                    if i >= 2:
                        dve.wait_ge(s[f"out_stored{i % 2}"], 16 * (i // 2))
                    b = 4 + 2 * (i % 2)
                    nc.vector.tensor_tensor(obuf[0:rows, i % 2, :], ps[0:rows, b:b + 2, :].rearrange("p b n -> p (b n)"),
                                            xres[0:rows, i % 2, :], ALU.add).then_inc(s["res_ready"], 1)

        @block.tensor
        def _(pe):
            pe.wait_ge(s["consts"], 6)
            for i, (n0, rows) in enumerate(LT):
                pe.wait_ge(s["h_ready"], i + 1)
                if i >= 2:
                    pe.wait_ge(s["hT_ready"], i - 1)
                for k in range(KT):
                    last = nc.tensor.transpose(ps[:, 2 * (i % 2) + k // 4, (k % 4) * P:(k % 4) * P + rows],
                                               hbuf[0:rows, i % 2, k * P:(k + 1) * P], ident[0:rows, 0:rows])
                last.then_inc(s["lnT_done"], 1)

            def root_block(n):
                c0, cols = NCOL[n]
                for m in range(KT):
                    bank = root_bank(n, m)
                    if n == 2 and m >= 6:
                        pe.wait_ge(s["root_evac"], 2 * KT + m - 5)
                    for k in range(KT):
                        last = nc.tensor.matmul(ps[:, bank, 0:cols], W[:, 0, k * D + m * P:k * D + (m + 1) * P],
                                                hT[:, k, c0:c0 + cols], start=(k == 0), stop=(k == KT - 1))
                    last.then_inc(s["u_done"], 1)

            pe.wait_ge(s["w_loaded0"], 16)
            pe.wait_ge(s["hT_ready"], len(LT))
            root_block(0)

            pe.wait_ge(s["root_evac"], KT)
            pe.wait_ge(s["scan_ready"], 1)
            hot3 = hot[0:EP].rearrange("p (g c) -> p g c", g=NG)
            scan3 = scan[0:EP].rearrange("p (g c) -> p g c", g=NG)
            nc.tensor.matmul(ps[0:NG, 0, 0:1], scan3[:, :, EC - 1], ones_bf[0:EP, 0:1], start=True,
                             stop=True).then_inc(s["totals_done"], 1)
            pe.wait_ge(s["ltile_ready"], 1)
            nc.tensor.matmul(ps[:, 1, 0:NG + 1], ltile[:, :], upper[:, :], start=True, stop=True).then_inc(s["bounds_done"], 1)
            for ch, (g0, gn) in enumerate(GCH):
                if ch >= 6:
                    pe.wait_ge(s["rank_used"], ch - 5)
                o = ps[0:EP, 2 + ch % 6, 0:gn * EC]
                nc.tensor.matmul(o, ones_bf[0:EP, 0:EP], scan[0:EP, g0 * EC:(g0 + gn) * EC], start=True, stop=False)
                nc.tensor.matmul(o, before[0:EP, 0:EP], hot[0:EP, g0 * EC:(g0 + gn) * EC], start=False,
                                 stop=True).then_inc(s["rank_done"], 1)
            pe.wait_ge(s["rank_used"], len(GCH))
            root_block(1)

            pe.wait_ge(s["root_evac"], 2 * KT)

            def table_step(c, b, first):
                pe.wait_ge(s["step_ready"], c + 1)
                for v in range(2):
                    last = nc.tensor.matmul(ps[:, v, 0:TMAX], lo_hot[0:EP, b, :], hi_val[0:EP, b, v, :], start=first,
                                            stop=True, skip_group_check=True)
                last.then_inc(s["step_used"], 1)

            for b in range(4):
                table_step(b, b, b == 0)
            with pe.Fori(1, EC // 4) as q:
                for b in range(4):
                    table_step(q * 4 + b, b, False)
            pe.wait_ge(s["step_used"], EC)
            nc.tensor.matmul(ps[:, 2, 0:2], lo_hot[0:EP, 0, :], hi_val[0:EP, 0, 0, 0:2], start=True,
                             stop=True).then_inc(s["table_done"], 1)
            root_block(2)

            pe.wait_ge(s["root_evac"], NU)
            pe.wait_ge(s["table_ready"], 1)

            def sum_tile(t, b, first):
                pe.wait_ge(s["tile_ready"], t + 1)
                slot = t % RING
                rows = G[:, :, :].rearrange("p b n -> p (b n)")
                hot_t = onehot[:, :, :].rearrange("p b n -> p (b n)")[:, bass.ds(slot * P, DT)]
                for half in range(2):
                    for part in range(2):
                        nc.tensor.matmul(ps[0:DT, 2 * b + half, :], hot_t,
                                         rows[:, bass.ds(slot * (2 * D) + (part * D + half * HC), HC)],
                                         start=first and part == 0, stop=True, skip_group_check=True)
                nc.tensor.matmul(ps[0:DT, 4 + 3 * b, 0:2], hot_t, ones_h[:, :], start=first, stop=True,
                                 skip_group_check=True).then_inc(s["tile_done"], 1)

            def sum_group(g, b, peeled):
                t0 = pe.value_load(bounds[0:1, bass.ds(g, 1)], min_val=0, max_val=TMAX - RING)
                t1 = pe.value_load(bounds[0:1, bass.ds(g + 1, 1)], min_val=2, max_val=TMAX - RING)
                if not peeled:
                    pe.wait_ge(s["natn_ready"], g - 1)
                sum_tile(t0, b, True)
                with pe.Fori(t0 + 1, t1) as t:
                    sum_tile(t, b, False)

            def turn_group(g, b, first):
                pe.wait_ge(s["natn_ready"], g + 1)
                if not first:
                    pe.wait_ge(s["meanT_ready"], g)
                for k in range(KT):
                    last = nc.tensor.transpose(ps[:, 5 + k // 4, (k % 4) * DT:(k % 4 + 1) * DT],
                                               natn[0:DT, b, k * P:(k + 1) * P], ident[0:DT, 0:DT])
                last.then_inc(s["meanT_done"], 1)

            sum_group(0, 0, True)
            sum_group(1, 1, True)
            turn_group(0, 0, True)
            with pe.Fori(1, NG // 2) as gp:
                sum_group(gp * 2, 0, False)
                turn_group(gp * 2 - 1, 1, False)
                sum_group(gp * 2 + 1, 1, False)
                turn_group(gp * 2, 0, False)
            turn_group(NG - 1, 1, False)

            pe.wait_ge(s["meanT_ready"], NG)

            def relation(r, par, wcount, mcount, first):
                pe.wait_ge(s[f"w_loaded{par}"], wcount)
                for n, (a, c) in enumerate(NB):
                    pe.wait_ge(s[f"mean_loaded{n}"], mcount)
                    mean = M[:, a * KT * DT:(a + c) * KT * DT].rearrange("p (j n) -> p j n", j=c)
                    for m in range(KT):
                        if not (first and n == 0):
                            pe.wait_ge(s["u_added"], r * NU + (n * KT + m - KT + 1))
                        for k in range(KT):
                            last = nc.tensor.matmul(ps[:, m, 0:c * DT].rearrange("p (j d) -> p j d", j=c),
                                                    W[:, par, k * D + m * P:k * D + (m + 1) * P],
                                                    mean[:, :, k * DT:(k + 1) * DT], start=(k == 0), stop=(k == KT - 1))
                        last.then_inc(s["main_done"], 1)

            relation(0, 1, 16, 16, True)
            relation(1, 0, 32, 32, False)
            with pe.Fori(1, R // 2) as rp:
                relation(rp * 2, 1, rp * 16 + 16, rp * 32 + 16, False)
                relation(rp * 2 + 1, 0, rp * 16 + 32, rp * 32 + 32, False)

            pe.wait_ge(s["u_added"], R * NU)
            pe.wait_ge(s["w_loaded1"], 16 * (R // 2 + 1))
            for n, (c0, cols) in enumerate(FB):
                for m in range(KT):
                    q = n * KT + m
                    if q >= 4:
                        pe.wait_ge(s["prod_ready"], q - 3)
                    for k in range(KT):
                        nc.tensor.matmul(ps[:, m % 4, 0:cols], W[:, 1, k * D + m * P:k * D + (m + 1) * P],
                                         uT[:, k, c0:c0 + cols], start=(k == 0), stop=False)
                    if q == 0:
                        pe.wait_ge(s["bot_loaded"], 32)
                    for k in range(KT):
                        last = nc.tensor.matmul(ps[:, m % 4, 0:cols], wbot[:, k, m * P:(m + 1) * P],
                                                hT[:, k, c0:c0 + cols], start=False, stop=(k == KT - 1))
                    last.then_inc(s["z_done"], 1)
                pe.wait_ge(s["gate_ready"], (n + 1) * KT)
                for i in range(c0 // P, (c0 + cols + P - 1) // P):
                    rows = LT[i][1]
                    if i >= 2:
                        pe.wait_ge(s["res_ready"], i - 1)
                    for k in range(KT):
                        last = nc.tensor.transpose(ps[0:rows, 4 + 2 * (i % 2) + k // 4, (k % 4) * P:(k % 4 + 1) * P],
                                                   gT[:, k, i * P - c0:i * P - c0 + rows], ident[:, :])
                    last.then_inc(s["gateT_done"], 1)


_INS = ['x', 'src', 'dst', 'edge_type_8', 'L0_gnn_weight', 'L0_gnn_root', 'L0_gnn_bias', 'L0_gnn_w_gate', 'L0_gnn_b_gate']


def kernel(**inputs):
    import numpy as _np
    import concourse.bacc as _bacc
    from concourse import mybir as _mybir
    from concourse.bass_utils import run_bass_kernel_spmd as _run

    nc = _bacc.Bacc("TRN2", target_bir_lowering=False, num_devices=1)
    arrays, args = {}, []
    for name in _INS:
        a = _np.ascontiguousarray(inputs[name])
        arrays[f"in_{name}_dram"] = a
        args.append(nc.dram_tensor(f"in_{name}_dram", a.shape, _mybir.dt.from_np(a.dtype), kind="ExternalInput").ap())
    shape = tuple(inputs['x'].shape)
    out = nc.dram_tensor("out_dram", shape, _mybir.dt.float32, kind="ExternalOutput").ap()
    gated_rgcn_preln(nc, *args, out)
    r = _run(nc, [arrays], core_ids=[0])
    return r.results[0]["out_dram"]
```
